# Optimizing a Trainium2 kernel written in Bass

```python
import numpy as np
import jax
import jax.numpy as jnp

def _softmax(x, axis=-1):
    return jax.nn.softmax(x, axis=axis)
def _gelu(x):
    return jax.nn.gelu(x, approximate=True)
def _silu(x):
    return jax.nn.silu(x)
def _sigmoid(x):
    return jax.nn.sigmoid(x)
def _layernorm(x, axis=-1, eps=1e-5):
    m = jnp.mean(x, axis=axis, keepdims=True)
    v = jnp.var(x, axis=axis, keepdims=True)
    return (x - m) / jnp.sqrt(v + eps)
def _scatter_add(tgt, idx, src, axis=0):
    return tgt.at[idx].add(src)
def _segment_sum(src, seg, n):
    return jax.ops.segment_sum(src, seg, n)

kernel_name = 'mk_conv_seq_d1_conv_nchw192_552333'

def setup_inputs(seed: int = 0):
    np.random.seed(seed)
    _w = jnp.asarray
    def _rec_inputs():
        import jax
        import jax.numpy as jnp
        _gk = jax.random.key(seed)
        x = -4.65e-05 + 0.9999 * jax.random.normal(jax.random.fold_in(_gk, 1), (4, 192, 256, 256), jnp.float32)
        return x
    x = _rec_inputs()
    def _L0_conv_setup():
        import jax, jax.numpy as jnp
        import numpy as np
        DIM = 192
        K = 3
        RED = 4
        B, H, W = (4, 256, 256)
        EPS = 1e-05

        def _make_mask():
            m = np.ones((DIM, 1, K, K), np.float32)
            m[:, :, K // 2, K // 2:] = 0.0
            m[:, :, K // 2 + 1:] = 0.0
            return jnp.asarray(m)
        MASK = _make_mask()
        key = jax.random.key(seed)
        ks = jax.random.split(key, 4)
        r = DIM // RED
        return {'x': jax.random.normal(ks[0], (B, DIM, H, W), jnp.float32), 'w1': jax.random.normal(ks[1], (r, DIM), jnp.float32) * 0.05, 'gamma': jnp.ones((r,), jnp.float32), 'beta': jnp.zeros((r,), jnp.float32), 'running_mean': jnp.zeros((r,), jnp.float32), 'running_var': jnp.ones((r,), jnp.float32), 'w2': jax.random.normal(ks[2], (DIM * K * K, r), jnp.float32) * 0.05, 'b2': jnp.zeros((DIM * K * K,), jnp.float32), 'bias': jnp.zeros((DIM,), jnp.float32)}
    _L0_conv_all = _L0_conv_setup()
    _L0_conv_in = {k: v for k, v in _L0_conv_all.items() if k in ('w1', 'gamma', 'beta', 'running_mean', 'running_var', 'w2', 'b2', 'bias', )}
    del _L0_conv_all

    return {
        "x": x,
        "L0_conv_w1": _L0_conv_in["w1"],
        "L0_conv_gamma": _L0_conv_in["gamma"],
        "L0_conv_beta": _L0_conv_in["beta"],
        "L0_conv_running_mean": _L0_conv_in["running_mean"],
        "L0_conv_running_var": _L0_conv_in["running_var"],
        "L0_conv_w2": _L0_conv_in["w2"],
        "L0_conv_b2": _L0_conv_in["b2"],
        "L0_conv_bias": _L0_conv_in["bias"],
    }

def reference(x, L0_conv_w1, L0_conv_gamma, L0_conv_beta, L0_conv_running_mean, L0_conv_running_var, L0_conv_w2, L0_conv_b2, L0_conv_bias):
    import jax
    import jax.numpy as jnp
    def _L0_conv_ref(x, w1, gamma, beta, running_mean, running_var, w2, b2, bias):
        import jax, jax.numpy as jnp
        import numpy as np
        DIM = 192
        K = 3
        RED = 4
        B, H, W = (4, 256, 256)
        EPS = 1e-05

        def _make_mask():
            m = np.ones((DIM, 1, K, K), np.float32)
            m[:, :, K // 2, K // 2:] = 0.0
            m[:, :, K // 2 + 1:] = 0.0
            return jnp.asarray(m)
        MASK = _make_mask()
        b, c, h, w = x.shape
        pooled = x.mean(axis=(2, 3))
        t = pooled @ w1.T
        t = gamma * (t - running_mean) * jax.lax.rsqrt(running_var + EPS) + beta
        t = jax.nn.relu(t)
        wt = t @ w2.T + b2
        wt = wt.reshape(b * DIM, 1, K, K) * jnp.tile(MASK, (b, 1, 1, 1))
        out = jax.lax.conv_general_dilated(x.reshape(1, b * c, h, w), wt, window_strides=(1, 1), padding=((1, 1), (1, 1)), feature_group_count=b * DIM, dimension_numbers=('NCHW', 'OIHW', 'NCHW'))
        out = out + jnp.tile(bias, (b,))[None, :, None, None]
        return out.reshape(b, c, h, w)

    def _gn(v, G=32, eps=1e-5):
        B_, C_, H_, W_ = v.shape
        g = v.reshape(B_, G, C_ // G, H_, W_)
        m = jnp.mean(g, axis=(2, 3, 4), keepdims=True)
        s = jnp.var(g, axis=(2, 3, 4), keepdims=True)
        return ((g - m) / jnp.sqrt(s + eps)).reshape(v.shape)

    def _ln_c(v, eps=1e-6):
        m = jnp.mean(v, axis=1, keepdims=True)
        s = jnp.var(v, axis=1, keepdims=True)
        return (v - m) / jnp.sqrt(s + eps)

    def _ln_t(v, eps=1e-5):
        m = jnp.mean(v, axis=-1, keepdims=True)
        s = jnp.var(v, axis=-1, keepdims=True)
        return (v - m) / jnp.sqrt(s + eps)

    def _to_tokens(v):
        B_, C_, H_, W_ = v.shape
        return v.reshape(B_, C_, H_ * W_).transpose(0, 2, 1)
    def _from_tokens(t, like):
        B_, C_, H_, W_ = like.shape
        return t.transpose(0, 2, 1).reshape(B_, C_, H_, W_)

    x = _L0_conv_ref(x, L0_conv_w1, L0_conv_gamma, L0_conv_beta, L0_conv_running_mean, L0_conv_running_var, L0_conv_w2, L0_conv_b2, L0_conv_bias)
    return x


_drawn_inputs = setup_inputs


def setup_inputs(seed=0):
    import zlib

    import numpy as np

    out = dict(_drawn_inputs(seed))
    spreads = {'L0_conv_gamma': (1.0, 0.2),
     'L0_conv_beta': (0.0, 0.1),
     'L0_conv_running_mean': (0.0, 0.1),
     'L0_conv_running_var': (1.0, 0.6),
     'L0_conv_b2': (0.0, 0.1),
     'L0_conv_bias': (0.0, 0.1)}
    factors = {'L0_conv_w1': 8.0}
    for name, (base, spread) in spreads.items():
        noise = np.random.default_rng([zlib.crc32(name.encode()), seed]).standard_normal(out[name].shape)
        drawn = base * np.exp(spread * noise) if base else spread * noise
        out[name] = jnp.asarray(drawn.astype(out[name].dtype))
    for name, factor in factors.items():
        out[name] = (out[name] * factor).astype(out[name].dtype)
    return out
```

```python
from contextlib import ExitStack

import numpy as np

import concourse.bass as bass
from concourse import mybir

F32 = mybir.dt.float32
U8 = mybir.dt.uint8
ALU = mybir.AluOpType
ACT = mybir.ActivationFunctionType

B, C, H, W = 4, 192, 256, 256
HID = C // 4
TAPS = 4
EPS = 1e-5
P = 128
ROWS = 8
BLK = H // ROWS
CPT = P // BLK
TPB = C // CPT
FREE = ROWS * W

STEPS = 4
GROUPS = TPB // STEPS
RES = 16
RP = 2
RC = 4
RO = 2
STREAM = TPB - RES
PE_ROWS = 5
NMAT = 5

G_RES = RES // STEPS
CHAIN_GROUPS = 2
ITEMS = [6] * G_RES + [4] * (GROUPS - G_RES - CHAIN_GROUPS) + [0] * CHAIN_GROUPS
assert sum(ITEMS) == TPB
FIRST = [sum(ITEMS[:g]) for g in range(GROUPS + 1)]


def spread(items):
    return [list(range(items * s // STEPS, items * (s + 1) // STEPS)) for s in range(STEPS)]


def runs():
    def kind(g):
        lo, hi = FIRST[g] + RP - 1, FIRST[g + 1] + RP - 1
        if ITEMS[g] == 0 or hi > TPB or lo < STREAM < hi:
            return ("alone", g)
        return (ITEMS[g], lo >= STREAM, g >= G_RES)
    out, g = [], 0
    while g < GROUPS:
        e = g + 1
        while e < GROUPS and kind(e) == kind(g):
            e += 1
        out.append((g, e))
        g = e
    return out


def conv_kernel(nc, x, w1, gamma, beta, mean, var, w2, b2, bias, out):
    x_t = x.rearrange("b c (k r) w -> (b c k r w)", r=ROWS).rearrange("(g p f) -> g p f", p=P, f=FREE)
    out_t = out.rearrange("b c (k r) w -> (b c k r w)", r=ROWS).rearrange("(g p f) -> g p f", p=P, f=FREE)

    with ExitStack() as ctx:
        def sb(name, shape, dt=F32):
            return ctx.enter_context(nc.sbuf_tensor(name, shape, dt))

        def sem(name):
            return ctx.enter_context(nc.semaphore(name))

        resident = sb("resident", [P, RES * FREE])
        pool_ring = sb("pool_ring", [P, RP * FREE])
        conv_ring = sb("conv_ring", [P, RC * FREE])
        out_ring = sb("out_ring", [P, RO * FREE])
        unused = sb("unused", [P, FREE], U8)
        sums = sb("sums", [P, TPB])
        w1_sb = sb("w1_sb", [TPB, CPT, HID])
        w2_sb = sb("w2_sb", [HID + 1, CPT, TPB * TAPS])
        masks = sb("masks", [P, 2, P])
        mats = sb("mats", [P, 2, NMAT, P])
        taps = sb("taps", [P, B * TPB * TAPS])
        bias_sb = sb("bias_sb", [P, TPB + 2])
        bias_now = sb("bias_now", [P, 2])
        chan = sb("chan", [P, CPT])
        pooled = sb("pooled", [TPB, CPT])
        bn = sb("bn", [HID, 8])
        h_sb = sb("h_sb", [HID + 1, BLK])
        GAMMA, BETA, MEAN, VAR, ROOT, RSTD, TMP, Z = (bn[:, i:i + 1] for i in range(8))

        conv_ps = [ctx.enter_context(nc.psum_tensor(f"conv_ps{i}", [P, 3 * 512], F32)) for i in range(2)]
        net_ps = ctx.enter_context(nc.psum_tensor("net_ps", [P, 512], F32))
        taps_ps = ctx.enter_context(nc.psum_tensor("taps_ps", [P, 512], F32))

        loaded = [sem(f"loaded{i}") for i in range(RP)]
        reloaded = [sem(f"reloaded{i}") for i in range(RC)]
        stored = [sem(f"stored{i}") for i in range(RO)]
        const_in = sem("const_in")
        masks_set = sem("masks_set")
        chan_set = sem("chan_set")
        bn_set = sem("bn_set")
        summed = sem("summed")
        mats_built = sem("mats_built")
        ps_full = sem("ps_full")
        started = sem("started")
        moved = sem("moved")
        tap0_in = sem("tap0_in")
        tap2_in = sem("tap2_in")
        conv_done = sem("conv_done")
        pooled_ps = sem("pooled_ps")
        pooled_sb = sem("pooled_sb")
        hid_ps = sem("hid_ps")
        z_set = sem("z_set")
        h_set = sem("h_set")
        taps_full = sem("taps_full")
        taps_set = sem("taps_set")

        def rows(t, lo, hi, c0=0, c1=W):
            return t.rearrange("p (r w) -> p r w", w=W)[:, lo:hi, c0:c1]

        def slot(ring, i):
            return ring[:, bass.ds(i * FREE, FREE)]

        def x_tile(g, s, gb):
            if gb:
                return slot(resident, g * STEPS + s)
            return slot(conv_ring, s % RC)

        def tap(n, k):
            return taps[:, bass.ds(n * TAPS + k, 1)]

        def schedule(eng, group, opening=None):
            def batch(b, kind):
                if opening and kind != "last":
                    opening(b)
                for lo, hi in runs():
                    if kind == "first" and lo == 0:
                        group(b, 0, lo, kind)
                        lo = 1
                    if hi - lo > 1:
                        with eng.Fori(lo, hi) as g:
                            group(b, g, lo, kind)
                    elif hi - lo == 1:
                        group(b, lo, lo, kind)
            batch(0, "first")
            with eng.Fori(1, B - 1) as b:
                batch(b, "middle")
            batch(B - 1, "last")

        block = ctx.enter_context(nc.Block())

        @block.sync
        def _(sp):
            def load0(g, s, tile, dst):
                sp.dma_start(dst, x_t[tile]).then_inc(reloaded[s], 16)

            for s in range(RC):
                load0(0, s, RES + s, slot(conv_ring, s))
            sp.dma_start(w1_sb[:, :, :], w1).then_inc(const_in, 16)
            sp.dma_start(w2_sb[0:HID, :, :], w2).then_inc(const_in, 16)
            sp.dma_start(w2_sb[HID:HID + 1, :, :], b2).then_inc(const_in, 16)
            for i, v in enumerate((gamma, beta, mean, var)):
                sp.dma_start(bn[:, i:i + 1], v.rearrange("(r a) -> r a", a=1)).then_inc(const_in, 16)
            for q in range(CPT):
                sp.dma_start(bias_sb[q * BLK:(q + 1) * BLK, :],
                             bias[q:q + 1, :].to_broadcast([BLK, TPB + 2])).then_inc(const_in, 16)
            with sp.Fori(1, STREAM // RC) as g:
                for s in range(RC):
                    sp.wait_ge(summed, (g - 1) * RC + s + 1)
                    load0(g, s, g * RC + s + RES, slot(conv_ring, s))
            with sp.Fori(0, RES // RC) as g:
                for s in range(RC):
                    sp.wait_ge(summed, g * RC + (STREAM - RC + s + 1))
                    load0(g, s, g * RC + s, slot(resident, g * RC + s))

            def store(n, s):
                sp.dma_start(out_t[n], slot(out_ring, s % RO)).then_inc(stored[s % RO], 16)

            def group(b, g, g0, kind):
                for s in range(STEPS):
                    n = b * TPB + g * STEPS + s
                    if not (kind == "first" and g0 == 0 and isinstance(g, int) and g == 0):
                        sp.wait_ge(conv_done, n - RC + 1)
                        store(n - RC, s)
                    if g0 >= G_RES:
                        if kind == "first" and g0 == G_RES:
                            sp.wait_ge(summed, STREAM)
                        sp.dma_start(slot(conv_ring, s), x_t[n]).then_inc(reloaded[s], 16)
            schedule(sp, group)
            for s in range(RC):
                n = B * TPB - RC + s
                sp.wait_ge(conv_done, n + 1)
                store(n, s)
            for s in range(RO):
                sp.wait_ge(stored[s], 16 * (B * TPB // RO))

        def reloads(b, g, s):
            return 16 * (TPB // RC + b * (STREAM // RC) + (g - G_RES) + 1)

        @block.gpsimd
        def _(gp):
            gp.memset(masks[:, :, :], 0.0).then_inc(masks_set, 1)
            gp.memset(h_sb[:, :], 1.0).then_inc(masks_set, 1)
            gp.wait_ge(masks_set, 2)
            for i in range(2):
                gp.affine_select(out=masks[:, i, :], in_=masks[:, i, :], compare_op=ALU.not_equal, fill=1.0,
                                 base=i, pattern=[[-1, P]], channel_multiplier=1).then_inc(masks_set, 1)
            gp.wait_ge(masks_set, 4)
            gp.memset(masks[:, 1, 0:P:BLK], 0.0).then_inc(masks_set, 1)
        MASKS_SET = 5
        CONSTS = 16 * (7 + CPT)

        def ready(eng):
            eng.wait_ge(masks_set, MASKS_SET)

        @block.scalar
        def _(act):
            act.wait_ge(bn_set, 1)
            act.activation(ROOT, TMP, ACT.Sqrt).then_inc(bn_set, 1)

            def pool(t, src, before):
                act.wait_ge(summed, before)
                act.activation(unused[:, :], src, ACT.Copy, accum_out=sums[:, bass.ds(t, 1)]).then_inc(summed, 1)

            def pool_first(g, s, stream):
                ready(act)
                act.wait_ge(reloaded[s], (g + 1) * 16)
                if stream:
                    pool(g * RC + s + RES, slot(conv_ring, s), g * RC + s)
                else:
                    pool(g * RC + s - STREAM, slot(resident, g * RC + s - STREAM), g * RC + s)

            for s in range(RC):
                pool_first(0, s, True)
            with act.Fori(1, STREAM // RC) as g:
                for s in range(RC):
                    pool_first(g, s, True)
            with act.Fori(STREAM // RC, TPB // RC) as g:
                for s in range(RC):
                    pool_first(g, s, False)

            def net_pooled(b):
                ready(act)
                act.wait_ge(pooled_ps, b + 1)
                act.activation(pooled[:, :], net_ps[0:TPB, 0:CPT], ACT.Copy, scale=1.0 / (H * W))\
                   .then_inc(pooled_sb, 1)

            def net_hidden(b):
                ready(act)
                act.wait_ge(z_set, b + 1)
                act.activation(h_sb[0:HID, :], Z.to_broadcast([HID, BLK]), ACT.Relu, bias=BETA)\
                   .then_inc(h_set, 1)

            def p1_load(b, item, par, is_stream, free_wait):
                if free_wait is not None:
                    act.wait_ge(summed, free_wait)
                if is_stream:
                    act.dma_start(slot(pool_ring, par), x_t[b * TPB + item + RES]).then_inc(loaded[par], 16)
                else:
                    act.wait_ge(conv_done, (b - 1) * TPB + (item - STREAM) + 1)
                    act.dma_start(slot(resident, item - STREAM), x_t[b * TPB + (item - STREAM)])\
                       .then_inc(loaded[par], 16)

            net_pooled(0)
            net_hidden(0)

            def opening(b):
                for j in range(RP - 1):
                    p1_load(b + 1, j, j % RP, True, (b + 1) * TPB)

            def pool_load(b, g0, first_item, j):
                ahead = FIRST[g0] + j + RP - 1
                item = first_item + j + RP - 1
                if ahead < TPB:
                    p1_load(b + 1, item, (j + RP - 1) % RP, ahead < STREAM, (b + 1) * TPB + item - RP + 1)

            def pool_item(b, g0, first_item, j):
                item = first_item + j
                ready(act)
                act.wait_ge(loaded[j % RP], (b * TPB + first_item) * (16 // RP) + 16 * (j // RP + 1))
                if j == 0 and g0 == 0:
                    act.wait_ge(pooled_ps, b + 1)
                if FIRST[g0] + j < STREAM:
                    pool(item + RES, slot(pool_ring, j % RP), (b + 1) * TPB + item)
                else:
                    pool(item - STREAM, slot(resident, item - STREAM), (b + 1) * TPB + item)

            def group(b, g, g0, kind):
                last = kind == "last"
                items = spread(0 if last else ITEMS[g0])
                first_item = FIRST[g0] + (g - g0) * ITEMS[g0]
                chain = [s + STEPS * (g0 - (GROUPS - CHAIN_GROUPS)) for s in range(STEPS)]
                for s in range(STEPS):
                    n = b * TPB + g * STEPS + s
                    if len(items[s]) == 2:
                        pool_load(b, g0, first_item, items[s][0])
                        pool_item(b, g0, first_item, items[s][0])
                        pool_load(b, g0, first_item, items[s][1])
                    elif items[s]:
                        pool_load(b, g0, first_item, items[s][0])
                    if chain[s] == 2 and not last:
                        net_pooled(b + 1)
                    if chain[s] == 4 and not last:
                        net_hidden(b + 1)
                    o = slot(out_ring, s % RO)
                    xt = x_tile(g, s, g0 < G_RES)
                    ready(act)
                    if s == 0 and g0 == 0:
                        act.wait_ge(taps_set, b + 1)
                    if not (kind == "first" and g0 == 0 and isinstance(g, int) and g == 0 and s < RO):
                        act.wait_ge(stored[s % RO], (b * TPB + g * STEPS) * (16 // RO) + 16 * (s // RO))
                    if g0 >= G_RES:
                        act.wait_ge(reloaded[s], reloads(b, g, s))
                    act.activation(rows(o, PE_ROWS, ROWS), rows(xt, PE_ROWS - 1, ROWS - 1), ACT.Identity,
                                   scale=tap(n, 1), bias=bias_sb[:, bass.ds(g * STEPS + s, 1)])\
                       .then_inc(started, 1)
                    act.wait_ge(ps_full, n + 1)
                    act.activation(o[:, 0:PE_ROWS * W], conv_ps[s % 2][:, W:W + PE_ROWS * W], ACT.Identity,
                                   bias=bias_now[:, s % 2:s % 2 + 1]).then_inc(moved, 1)
                    if items[s]:
                        pool_item(b, g0, first_item, items[s][-1])
            schedule(act, group, opening)

        @block.tensor
        def _(pe):
            def mm(out_ap, lhsT, rhs, start, stop):
                return nc.tensor.matmul(out_ap, lhsT, rhs, start=start, stop=stop)

            def net_mean(b):
                ready(pe)
                pe.wait_ge(summed, (b + 1) * TPB)
                mm(net_ps[0:TPB, 0:CPT], sums[:, :], chan[:, :], True, True).then_inc(pooled_ps, 1)

            def net_w1(b):
                ready(pe)
                pe.wait_ge(pooled_sb, b + 1)
                for q in range(CPT):
                    last = mm(net_ps[0:HID, 8:9], w1_sb[:, q, :], pooled[:, q:q + 1], q == 0, q == CPT - 1)
                last.then_inc(hid_ps, 1)

            def net_w2(b):
                ready(pe)
                pe.wait_ge(h_set, b + 1)
                for q in range(CPT):
                    last = mm(taps_ps[q * BLK:(q + 1) * BLK, 0:TPB * TAPS], h_sb[:, :], w2_sb[:, q, :], True, True)
                last.then_inc(taps_full, 1)

            pe.wait_ge(const_in, CONSTS)
            pe.wait_ge(masks_set, MASKS_SET)
            pe.wait_ge(chan_set, 1 + CPT)
            net_mean(0)
            net_w1(0)
            net_w2(0)

            def group(b, g, g0, kind):
                for s in range(STEPS):
                    n = b * TPB + g * STEPS + s
                    chain = s + STEPS * (g0 - (GROUPS - CHAIN_GROUPS))
                    if kind != "last":
                        if chain == 1:
                            net_mean(b + 1)
                        if chain == 3:
                            net_w1(b + 1)
                        if chain == 5:
                            net_w2(b + 1)
                    ps = conv_ps[s % 2]
                    xt = x_tile(g, s, g0 < G_RES)
                    d0, d1, s0, s1, s2 = (mats[:, s % 2, i, :] for i in range(NMAT))
                    pe.wait_ge(mats_built, n + 1)
                    if g0 >= G_RES:
                        pe.wait_ge(reloaded[s], reloads(b, g, s))
                    if not (kind == "first" and g0 == 0 and isinstance(g, int) and g == 0 and s < 2):
                        pe.wait_ge(moved, n - 1)
                    mm(ps[:, W:2 * W], s1, xt[:, 7 * W:8 * W], True, False)
                    mm(ps[:, W + 1:2 * W], s0, xt[:, 7 * W:8 * W - 1], False, False)
                    mm(ps[:, W:2 * W - 1], s2, xt[:, 7 * W + 1:8 * W], False, True)
                    for r in range(1, PE_ROWS, 2):
                        o = ps[:, W + r * W:W + (r + 2) * W]
                        mm(o, d1, xt[:, (r - 1) * W:(r + 1) * W], True, False)
                        last = mm(rows(o, 0, 2, 1, W), d0, rows(xt, r - 1, r + 1, 0, W - 1), False, True)
                    last.then_inc(ps_full, 1)
            schedule(pe, group)

        @block.vector
        def _(dve):
            V = nc.vector
            V.memset(chan[:, :], 0.0).then_inc(chan_set, 1)
            dve.wait_ge(chan_set, 1)
            for q in range(CPT):
                V.memset(chan[q * BLK:(q + 1) * BLK, q:q + 1], 1.0).then_inc(chan_set, 1)
            dve.wait_ge(const_in, CONSTS)
            V.tensor_scalar(TMP, VAR, EPS, None, ALU.add).then_inc(bn_set, 1)
            dve.wait_ge(bn_set, 2)
            V.reciprocal(RSTD, ROOT).then_inc(bn_set, 1)
            dve.wait_ge(bn_set, 3)
            V.tensor_tensor(ROOT, RSTD, RSTD, ALU.mult).then_inc(bn_set, 1)
            dve.wait_ge(bn_set, 4)
            V.tensor_tensor(ROOT, ROOT, TMP, ALU.mult).then_inc(bn_set, 1)
            dve.wait_ge(bn_set, 5)
            V.tensor_scalar(ROOT, ROOT, -0.5, 1.5, ALU.mult, ALU.add).then_inc(bn_set, 1)
            dve.wait_ge(bn_set, 6)
            V.tensor_tensor(RSTD, RSTD, ROOT, ALU.mult).then_inc(bn_set, 1)
            dve.wait_ge(bn_set, 7)
            V.tensor_tensor(GAMMA, GAMMA, RSTD, ALU.mult).then_inc(bn_set, 1)

            def net_norm(b):
                dve.wait_ge(hid_ps, b + 1)
                V.tensor_scalar(Z, net_ps[0:HID, 8:9], MEAN, GAMMA, ALU.subtract, ALU.mult).then_inc(z_set, 1)

            def net_taps(b):
                dve.wait_ge(taps_full, b + 1)
                V.tensor_copy(taps[:, bass.ds(b * (TPB * TAPS), TPB * TAPS)], taps_ps[:, 0:TPB * TAPS])\
                 .then_inc(taps_set, 1)

            def build(n, t, par):
                V.tensor_copy(bias_now[:, par:par + 1], bias_sb[:, bass.ds(t, 1)])
                for i, (m, k) in enumerate(((0, 0), (0, 1), (1, 0), (1, 1), (1, 2))):
                    last = V.tensor_scalar(mats[:, par, i, :], masks[:, m, :], tap(n, k), None, ALU.mult)
                last.then_inc(mats_built, 1)

            dve.wait_ge(masks_set, MASKS_SET)
            dve.wait_ge(bn_set, 8)
            net_norm(0)
            net_taps(0)
            dve.wait_ge(taps_set, 1)
            build(0, 0, 0)
            build(1, 1, 1)

            def add_tap(o, xr, n, k):
                return V.scalar_tensor_tensor(o, xr, tap(n, k), o, ALU.mult, ALU.add)

            def group(b, g, g0, kind):
                for s in range(STEPS):
                    n = b * TPB + g * STEPS + s
                    chain = s + STEPS * (g0 - (GROUPS - CHAIN_GROUPS))
                    if kind != "last":
                        if chain == 4:
                            net_norm(b + 1)
                        if chain == 6:
                            net_taps(b + 1)
                            dve.wait_ge(taps_set, b + 2)
                    o = slot(out_ring, s % RO)
                    xt = x_tile(g, s, g0 < G_RES)
                    dve.wait_ge(started, n + 1)
                    add_tap(rows(o, PE_ROWS, ROWS, 1, W), rows(xt, PE_ROWS - 1, ROWS - 1, 0, W - 1), n, 0)\
                        .then_inc(tap0_in, 1)
                    dve.wait_ge(moved, n + 1)
                    dve.wait_ge(tap0_in, n + 1)
                    add_tap(rows(o, 1, ROWS, 0, W - 1), rows(xt, 0, ROWS - 1, 1, W), n, 2).then_inc(tap2_in, 1)
                    if not (kind == "last" and chain >= 6):
                        build(n + 2, g * STEPS + s + 2, s % 2)
                    dve.wait_ge(tap2_in, n + 1)
                    add_tap(rows(o, 0, ROWS, 1, W), rows(xt, 0, ROWS, 0, W - 1), n, 3).then_inc(conv_done, 1)
            schedule(dve, group)


_OUT = (B, C, H, W)


def kernel(**inputs):
    import concourse.bacc as bacc
    from concourse.bass_utils import run_bass_kernel_spmd

    a = {k.replace("L0_conv_", ""): np.asarray(v) for k, v in inputs.items()}
    w1 = np.ascontiguousarray(a["w1"].T.reshape(TPB, CPT, HID))
    w2 = a["w2"].reshape(TPB, CPT, 9, HID)[:, :, :TAPS, :]
    w2 = np.ascontiguousarray(w2.transpose(3, 1, 0, 2).reshape(HID, CPT, TPB * TAPS))
    b2 = a["b2"].reshape(TPB, CPT, 9)[:, :, :TAPS]
    b2 = np.ascontiguousarray(b2.transpose(1, 0, 2).reshape(1, CPT, TPB * TAPS))
    bias = a["bias"].reshape(TPB, CPT).T
    bias = np.ascontiguousarray(np.concatenate([bias, bias[:, :2]], axis=1))
    arrays = {"x": np.ascontiguousarray(a["x"]), "w1": w1, "gamma": a["gamma"], "beta": a["beta"],
              "mean": a["running_mean"], "var": a["running_var"], "w2": w2, "b2": b2, "bias": bias}

    nc = bacc.Bacc("TRN2", target_bir_lowering=False, num_devices=1)
    aps = [nc.dram_tensor(f"{k}_dram", v.shape, mybir.dt.from_np(v.dtype), kind="ExternalInput").ap()
           for k, v in arrays.items()]
    out = nc.dram_tensor("out_dram", _OUT, F32, kind="ExternalOutput").ap()
    conv_kernel(nc, *aps, out)
    r = run_bass_kernel_spmd(nc, [{f"{k}_dram": v for k, v in arrays.items()}], core_ids=[0])
    return r.results[0]["out_dram"]
```

```python
from contextlib import ExitStack

import numpy as np

import concourse.bass as bass
from concourse import mybir

F32 = mybir.dt.float32
U8 = mybir.dt.uint8
ALU = mybir.AluOpType
ACT = mybir.ActivationFunctionType

B, C, H, W = 4, 192, 256, 256
HID = C // 4
TAPS = 4
EPS = 1e-5
P = 128
ROWS = 8
BLK = H // ROWS
CPT = P // BLK
TPB = C // CPT
FREE = ROWS * W

STEPS = 4
GROUPS = TPB // STEPS
RES = 16
RP = 2
RC = 4
HALF = ROWS // 2
RO = 2
STREAM = TPB - RES
NMAT = 5

G_RES = RES // STEPS
CHAIN_GROUPS = 2
ITEMS = [6] * G_RES + [4] * (GROUPS - G_RES - CHAIN_GROUPS) + [0] * CHAIN_GROUPS
assert sum(ITEMS) == TPB
FIRST = [sum(ITEMS[:g]) for g in range(GROUPS + 1)]


def spread(items):
    return [list(range(items * s // STEPS, items * (s + 1) // STEPS)) for s in range(STEPS)]


def runs():
    def kind(g):
        lo, hi = FIRST[g] + RP - 1, FIRST[g + 1] + RP - 1
        if g == 0 or ITEMS[g] == 0 or hi > TPB or lo < STREAM < hi:
            return ("alone", g)
        return (ITEMS[g], lo >= STREAM, g >= G_RES)
    out, g = [], 0
    while g < GROUPS:
        e = g + 1
        while e < GROUPS and kind(e) == kind(g):
            e += 1
        out.append((g, e))
        g = e
    return out


def conv_kernel(nc, x, w1, gamma, beta, mean, var, w2, b2, bias, out):
    x_t = x.rearrange("b c (k r) w -> (b c k r w)", r=ROWS).rearrange("(g p f) -> g p f", p=P, f=FREE)
    out_t = out.rearrange("b c (k r) w -> (b c k r w)", r=ROWS).rearrange("(g p f) -> g p f", p=P, f=FREE)

    with ExitStack() as ctx:
        def sb(name, shape, dt=F32):
            return ctx.enter_context(nc.sbuf_tensor(name, shape, dt))

        def sem(name):
            return ctx.enter_context(nc.semaphore(name))

        resident = sb("resident", [P, RES * FREE])
        pool_ring = sb("pool_ring", [P, RP * FREE])
        conv_ring = sb("conv_ring", [P, RC * FREE])
        out_ring = sb("out_ring", [P, RO * FREE])
        unused = sb("unused", [P, FREE], U8)
        sums = sb("sums", [P, TPB])
        w1_sb = sb("w1_sb", [TPB, CPT, HID])
        w2_sb = sb("w2_sb", [HID + 1, CPT, TPB * TAPS])
        masks = sb("masks", [P, 2 * P])
        mats = sb("mats", [P, 2, NMAT * P])
        taps = sb("taps", [P, B * TPB * TAPS])
        bias_sb = sb("bias_sb", [P, TPB + 2])
        bias_now = sb("bias_now", [P, 2])
        chan = sb("chan", [P, CPT])
        pooled = sb("pooled", [TPB, CPT])
        bn = sb("bn", [HID, 8])
        h_sb = sb("h_sb", [HID + 1, BLK])
        GAMMA, BETA, MEAN, VAR, ROOT, RSTD, VAR_EPS, SHIFT = (bn[:, i:i + 1] for i in range(8))

        conv_ps = [ctx.enter_context(nc.psum_tensor(f"conv_ps{i}", [P, 3 * 512], F32)) for i in range(2)]
        net_ps = ctx.enter_context(nc.psum_tensor("net_ps", [P, 512], F32))
        taps_ps = ctx.enter_context(nc.psum_tensor("taps_ps", [P, 512], F32))

        loaded = [sem(f"loaded{i}") for i in range(RP)]
        reloaded = [sem(f"reloaded{i}") for i in range(RC)]
        stored = [[sem(f"stored_{'AB'[h]}{i}") for h in range(2)] for i in range(RO)]
        const_in = sem("const_in")
        masks_set = sem("masks_set")
        chan_set = sem("chan_set")
        bn_set = sem("bn_set")
        bias_set = sem("bias_set")
        summed = sem("summed")
        mats_built = sem("mats_built")
        ps_full = sem("ps_full")
        moved = sem("moved")
        started = sem("started")
        tap2_a = sem("tap2_a")
        tap0_b = sem("tap0_b")
        tap2_b = sem("tap2_b")
        conv_done = sem("conv_done")
        pooled_ps = sem("pooled_ps")
        pooled_sb = sem("pooled_sb")
        hid_ps = sem("hid_ps")
        h_set = sem("h_set")
        taps_full = sem("taps_full")
        taps_set = sem("taps_set")

        def rows(t, lo, hi, c0=0, c1=W):
            return t.rearrange("p (r w) -> p r w", w=W)[:, lo:hi, c0:c1]

        def slot(ring, i):
            return ring[:, bass.ds(i * FREE, FREE)]

        def out_half(s, h):
            lo = (s % RO) * FREE + h * HALF * W
            return out_ring[:, lo:lo + HALF * W]

        def x_tile(g, s, gb):
            if gb:
                return slot(resident, g * STEPS + s)
            return slot(conv_ring, s % RC)

        def tap(n, k):
            return taps[:, bass.ds(n * TAPS + k, 1)]

        def schedule(eng, group, opening=None):
            def batch(b, kind):
                if opening and kind != "last":
                    opening(b, kind)
                for lo, hi in runs():
                    if hi - lo > 1:
                        with eng.Fori(lo, hi) as g:
                            group(b, g, lo, kind)
                    elif hi - lo == 1:
                        group(b, lo, lo, kind)
            batch(0, "first")
            with eng.Fori(1, B - 1) as b:
                batch(b, "middle")
            batch(B - 1, "last")

        block = ctx.enter_context(nc.Block())

        @block.sync
        def _(sp):
            def load0(g, s, tile, dst):
                sp.dma_start(dst, x_t[tile]).then_inc(reloaded[s], 16)

            for s in range(RC):
                load0(0, s, RES + s, slot(conv_ring, s))
            sp.dma_start(w1_sb[:, :, :], w1).then_inc(const_in, 16)
            sp.dma_start(w2_sb[0:HID, :, :], w2).then_inc(const_in, 16)
            sp.dma_start(w2_sb[HID:HID + 1, :, :], b2).then_inc(const_in, 16)
            for i, v in enumerate((gamma, beta, mean, var)):
                sp.dma_start(bn[:, i:i + 1], v.rearrange("(r a) -> r a", a=1)).then_inc(const_in, 16)
            for q in range(CPT):
                sp.dma_start(bias_sb[q * BLK:(q + 1) * BLK, :],
                             bias[q:q + 1, :].to_broadcast([BLK, TPB + 2])).then_inc(const_in, 16)
            with sp.Fori(1, STREAM // RC) as g:
                for s in range(RC):
                    sp.wait_ge(summed, (g - 1) * RC + s + 1)
                    load0(g, s, g * RC + s + RES, slot(conv_ring, s))
            with sp.Fori(0, RES // RC) as g:
                for s in range(RC):
                    sp.wait_ge(summed, g * RC + (STREAM - RC + s + 1))
                    load0(g, s, g * RC + s, slot(resident, g * RC + s))

            def store(n, s):
                for h in range(2):
                    sp.wait_ge(conv_done, n * 2 + h + 1)
                    sp.dma_start(out_t[n][:, h * HALF * W:(h + 1) * HALF * W], out_half(s, h))\
                      .then_inc(stored[s % RO][h], 16)

            def group(b, g, g0, kind):
                for s in range(STEPS):
                    n = b * TPB + g * STEPS + s
                    if not (kind == "first" and g0 == 0 and isinstance(g, int) and g == 0):
                        store(n - RC, s)
                    if g0 == 0:
                        if kind == "first":
                            sp.wait_ge(summed, TPB - RC + s + 1)
                        sp.dma_start(slot(conv_ring, s), x_t[n + RES]).then_inc(reloaded[s], 16)
                    elif g0 > G_RES:
                        sp.dma_start(slot(conv_ring, s), x_t[n]).then_inc(reloaded[s], 16)
            schedule(sp, group)
            for s in range(RC):
                store(B * TPB - RC + s, s)
            for s in range(RO):
                for h in range(2):
                    sp.wait_ge(stored[s][h], 16 * (B * TPB // RO))

        def reloads(b, g, s):
            return 16 * (TPB // RC + b * (STREAM // RC) + (g - G_RES) + 1)

        @block.gpsimd
        def _(gp):
            gp.memset(masks[:, :], 0.0).then_inc(masks_set, 1)
            gp.memset(h_sb[:, :], 1.0).then_inc(masks_set, 1)
            gp.wait_ge(masks_set, 2)
            for i in range(2):
                m = masks[:, i * P:(i + 1) * P]
                gp.affine_select(out=m, in_=m, compare_op=ALU.not_equal, fill=1.0, base=i,
                                 pattern=[[-1, P]], channel_multiplier=1).then_inc(masks_set, 1)
            gp.wait_ge(masks_set, 4)
            gp.memset(masks[:, P:2 * P:BLK], 0.0).then_inc(masks_set, 1)
        MASKS_SET = 5
        CONSTS = 16 * (7 + CPT)

        def ready(eng):
            eng.wait_ge(masks_set, MASKS_SET)

        @block.scalar
        def _(act):
            act.wait_ge(bn_set, 1)
            act.activation(ROOT, VAR_EPS, ACT.Sqrt).then_inc(bn_set, 1)

            def pool(t, src, before):
                act.wait_ge(summed, before)
                act.activation(unused[:, :], src, ACT.Copy, accum_out=sums[:, bass.ds(t, 1)]).then_inc(summed, 1)

            def pool_first(g, s, stream):
                ready(act)
                act.wait_ge(reloaded[s], (g + 1) * 16)
                if stream:
                    pool(g * RC + s + RES, slot(conv_ring, s), g * RC + s)
                else:
                    pool(g * RC + s - STREAM, slot(resident, g * RC + s - STREAM), g * RC + s)

            for s in range(RC):
                pool_first(0, s, True)
            with act.Fori(1, STREAM // RC) as g:
                for s in range(RC):
                    pool_first(g, s, True)
            with act.Fori(STREAM // RC, TPB // RC) as g:
                for s in range(RC):
                    pool_first(g, s, False)

            def net_pooled(b):
                act.wait_ge(pooled_ps, b + 1)
                act.activation(pooled[:, :], net_ps[0:TPB, 0:CPT], ACT.Copy, scale=1.0 / (H * W))\
                   .then_inc(pooled_sb, 1)

            def net_hidden(b):
                act.wait_ge(hid_ps, b + 1)
                act.activation(h_sb[0:HID, :], net_ps[0:HID, 8:9].to_broadcast([HID, BLK]), ACT.Relu,
                               scale=GAMMA, bias=SHIFT).then_inc(h_set, 1)

            def net_taps(b):
                act.activation(taps[:, bass.ds(b * (TPB * TAPS), TPB * TAPS)], taps_ps[:, 0:TPB * TAPS],
                               ACT.Copy).then_inc(taps_set, 1)

            def build(n, par):
                act.activation(mats[:, par, 0:2 * P], masks[:, :], ACT.Copy, scale=tap(n, 0))
                act.activation(mats[:, par, 2 * P:4 * P], masks[:, :], ACT.Copy, scale=tap(n, 1))
                act.activation(mats[:, par, 4 * P:5 * P], masks[:, P:2 * P], ACT.Copy, scale=tap(n, 2))\
                   .then_inc(mats_built, 1)

            def p1_load(b, item, par, is_stream, free_wait):
                if free_wait is not None:
                    act.wait_ge(summed, free_wait)
                if is_stream:
                    act.dma_start(slot(pool_ring, par), x_t[b * TPB + item + RES]).then_inc(loaded[par], 16)
                else:
                    act.wait_ge(conv_done, ((b - 1) * TPB + (item - STREAM) + 1) * 2)
                    act.dma_start(slot(resident, item - STREAM), x_t[b * TPB + (item - STREAM)])\
                       .then_inc(loaded[par], 16)

            def opening(b, kind):
                if kind != "first":
                    for j in range(RP - 1):
                        p1_load(b + 1, j, j % RP, True, (b + 1) * TPB)

            opening(0, "early")
            act.wait_ge(bias_set, 1)
            act.wait_ge(bn_set, 10)
            net_pooled(0)
            net_hidden(0)
            act.wait_ge(taps_full, 1)
            net_taps(0)
            act.wait_ge(taps_set, 1)
            build(0, 0)
            build(1, 1)

            def pool_load(b, g0, first_item, j):
                ahead = FIRST[g0] + j + RP - 1
                item = first_item + j + RP - 1
                if ahead < TPB:
                    p1_load(b + 1, item, (j + RP - 1) % RP, ahead < STREAM, (b + 1) * TPB + item - RP + 1)

            def pool_item(b, g0, first_item, j):
                item = first_item + j
                ready(act)
                act.wait_ge(loaded[j % RP], (b * TPB + first_item) * (16 // RP) + 16 * (j // RP + 1))
                if j == 0 and g0 == 0:
                    act.wait_ge(pooled_ps, b + 1)
                if FIRST[g0] + j < STREAM:
                    pool(item + RES, slot(pool_ring, j % RP), (b + 1) * TPB + item)
                else:
                    pool(item - STREAM, slot(resident, item - STREAM), (b + 1) * TPB + item)

            def group(b, g, g0, kind):
                last = kind == "last"
                items = spread(0 if last else ITEMS[g0])
                first_item = FIRST[g0] + (g - g0) * ITEMS[g0]
                chain = [s + STEPS * (g0 - (GROUPS - CHAIN_GROUPS)) for s in range(STEPS)]
                for s in range(STEPS):
                    n = b * TPB + g * STEPS + s
                    if len(items[s]) == 2:
                        pool_load(b, g0, first_item, items[s][0])
                        pool_item(b, g0, first_item, items[s][0])
                        pool_load(b, g0, first_item, items[s][1])
                    elif items[s]:
                        pool_load(b, g0, first_item, items[s][0])
                    if chain[s] == 2 and not last:
                        net_pooled(b + 1)
                    if chain[s] == 4 and not last:
                        net_hidden(b + 1)
                    xt = x_tile(g, s, g0 < G_RES)
                    if not (kind == "first" and g0 == 0 and s < RO):
                        for h in range(2):
                            act.wait_ge(stored[s % RO][h], (b * TPB + g * STEPS) * (16 // RO) + 16 * (s // RO))
                    if chain[s] == 5 and not last:
                        act.wait_ge(taps_full, b + 2)
                    if chain[s] == 6 and not last:
                        act.wait_ge(taps_set, b + 2)
                    act.wait_ge(ps_full, n + 1)
                    act.activation(out_half(s, 0), conv_ps[s % 2][:, W:W + HALF * W], ACT.Identity,
                                   bias=bias_now[:, s % 2:s % 2 + 1]).then_inc(moved, 1)
                    act.activation(out_half(s, 1), xt[:, (HALF - 1) * W:(ROWS - 1) * W], ACT.Identity,
                                   scale=tap(n, 1), bias=bias_now[:, s % 2:s % 2 + 1]).then_inc(started, 1)
                    if chain[s] == 5 and not last:
                        net_taps(b + 1)
                    if not (last and chain[s] >= 6):
                        build(n + 2, s % 2)
                    if items[s]:
                        pool_item(b, g0, first_item, items[s][-1])
            schedule(act, group, opening)

        @block.tensor
        def _(pe):
            def mm(out_ap, lhsT, rhs, start, stop):
                return nc.tensor.matmul(out_ap, lhsT, rhs, start=start, stop=stop)

            def net_mean(b):
                ready(pe)
                pe.wait_ge(summed, (b + 1) * TPB)
                mm(net_ps[0:TPB, 0:CPT], sums[:, :], chan[:, :], True, True).then_inc(pooled_ps, 1)

            def net_w1(b):
                ready(pe)
                pe.wait_ge(pooled_sb, b + 1)
                for q in range(CPT):
                    last = mm(net_ps[0:HID, 8:9], w1_sb[:, q, :], pooled[:, q:q + 1], q == 0, q == CPT - 1)
                last.then_inc(hid_ps, 1)

            def net_w2(b):
                ready(pe)
                pe.wait_ge(h_set, b + 1)
                for q in range(CPT):
                    last = mm(taps_ps[q * BLK:(q + 1) * BLK, 0:TPB * TAPS], h_sb[:, :], w2_sb[:, q, :], True, True)
                last.then_inc(taps_full, 1)

            pe.wait_ge(const_in, CONSTS)
            pe.wait_ge(masks_set, MASKS_SET)
            pe.wait_ge(chan_set, 1 + CPT)
            net_mean(0)
            net_w1(0)
            net_w2(0)

            def group(b, g, g0, kind):
                for s in range(STEPS):
                    n = b * TPB + g * STEPS + s
                    chain = s + STEPS * (g0 - (GROUPS - CHAIN_GROUPS))
                    if kind != "last":
                        if chain == 1:
                            net_mean(b + 1)
                        if chain == 3:
                            net_w1(b + 1)
                        if chain == 5:
                            net_w2(b + 1)
                    ps = conv_ps[s % 2]
                    xt = x_tile(g, s, g0 < G_RES)
                    d0, s0, d1, s1, s2 = (mats[:, s % 2, i * P:(i + 1) * P] for i in range(NMAT))
                    pe.wait_ge(mats_built, n + 1)
                    if g0 >= G_RES:
                        pe.wait_ge(reloaded[s], reloads(b, g, s))
                    if not (kind == "first" and g0 == 0 and isinstance(g, int) and g == 0 and s < 2):
                        pe.wait_ge(moved, n - 1)
                    mm(ps[:, W:2 * W], s1, xt[:, 7 * W:8 * W], True, False)
                    mm(ps[:, W + 1:2 * W], s0, xt[:, 7 * W:8 * W - 1], False, False)
                    mm(ps[:, W:2 * W - 1], s2, xt[:, 7 * W + 1:8 * W], False, True)
                    for r, k in ((1, 2), (3, 1)):
                        o = ps[:, W + r * W:W + (r + k) * W]
                        mm(o, d1, xt[:, (r - 1) * W:(r + k - 1) * W], True, False)
                        last = mm(rows(o, 0, k, 1, W), d0, rows(xt, r - 1, r + k - 1, 0, W - 1), False, True)
                    last.then_inc(ps_full, 1)
            schedule(pe, group)

        @block.vector
        def _(dve):
            V = nc.vector
            V.memset(chan[:, :], 0.0).then_inc(chan_set, 1)
            dve.wait_ge(chan_set, 1)
            for q in range(CPT):
                V.memset(chan[q * BLK:(q + 1) * BLK, q:q + 1], 1.0).then_inc(chan_set, 1)
            dve.wait_ge(const_in, CONSTS)
            V.tensor_scalar(VAR_EPS, VAR, EPS, None, ALU.add).then_inc(bn_set, 1)
            dve.wait_ge(bn_set, 2)
            V.reciprocal(RSTD, ROOT).then_inc(bn_set, 1)
            dve.wait_ge(bn_set, 3)
            V.tensor_tensor(ROOT, RSTD, RSTD, ALU.mult).then_inc(bn_set, 1)
            dve.wait_ge(bn_set, 4)
            V.tensor_tensor(ROOT, ROOT, VAR_EPS, ALU.mult).then_inc(bn_set, 1)
            dve.wait_ge(bn_set, 5)
            V.tensor_scalar(ROOT, ROOT, -0.5, 1.5, ALU.mult, ALU.add).then_inc(bn_set, 1)
            dve.wait_ge(bn_set, 6)
            V.tensor_tensor(RSTD, RSTD, ROOT, ALU.mult).then_inc(bn_set, 1)
            dve.wait_ge(bn_set, 7)
            V.tensor_tensor(GAMMA, GAMMA, RSTD, ALU.mult).then_inc(bn_set, 1)
            dve.wait_ge(bn_set, 8)
            V.tensor_tensor(SHIFT, MEAN, GAMMA, ALU.mult).then_inc(bn_set, 1)
            dve.wait_ge(bn_set, 9)
            V.tensor_tensor(SHIFT, BETA, SHIFT, ALU.subtract).then_inc(bn_set, 1)

            def now(t, par):
                V.tensor_copy(bias_now[:, par:par + 1], bias_sb[:, bass.ds(t, 1)])

            now(0, 0)
            V.tensor_copy(bias_now[:, 1:2], bias_sb[:, 1:2]).then_inc(bias_set, 1)

            def add_tap(o, xr, n, k):
                return V.scalar_tensor_tensor(o, xr, tap(n, k), o, ALU.mult, ALU.add)

            def group(b, g, g0, kind):
                for s in range(STEPS):
                    n = b * TPB + g * STEPS + s
                    if g0 == 0 and s == 0:
                        dve.wait_ge(taps_set, b + 1)
                    oa, ob = out_half(s, 0), out_half(s, 1)
                    xt = x_tile(g, s, g0 < G_RES)
                    dve.wait_ge(moved, n + 1)
                    add_tap(rows(oa, 1, HALF, 0, W - 1), rows(xt, 0, HALF - 1, 1, W), n, 2).then_inc(tap2_a, 1)
                    dve.wait_ge(started, n + 1)
                    add_tap(rows(ob, 0, HALF, 1, W), rows(xt, HALF - 1, ROWS - 1, 0, W - 1), n, 0)\
                        .then_inc(tap0_b, 1)
                    dve.wait_ge(tap2_a, n + 1)
                    add_tap(rows(oa, 0, HALF, 1, W), rows(xt, 0, HALF, 0, W - 1), n, 3).then_inc(conv_done, 1)
                    dve.wait_ge(tap0_b, n + 1)
                    add_tap(rows(ob, 0, HALF, 0, W - 1), rows(xt, HALF - 1, ROWS - 1, 1, W), n, 2)\
                        .then_inc(tap2_b, 1)
                    now(g * STEPS + s + 2, s % 2)
                    dve.wait_ge(tap2_b, n + 1)
                    add_tap(rows(ob, 0, HALF, 1, W), rows(xt, HALF, ROWS, 0, W - 1), n, 3).then_inc(conv_done, 1)
            schedule(dve, group)


_OUT = (B, C, H, W)


def kernel(**inputs):
    import concourse.bacc as bacc
    from concourse.bass_utils import run_bass_kernel_spmd

    a = {k.replace("L0_conv_", ""): np.asarray(v) for k, v in inputs.items()}
    w1 = np.ascontiguousarray(a["w1"].T.reshape(TPB, CPT, HID))
    w2 = a["w2"].reshape(TPB, CPT, 9, HID)[:, :, :TAPS, :]
    w2 = np.ascontiguousarray(w2.transpose(3, 1, 0, 2).reshape(HID, CPT, TPB * TAPS))
    b2 = a["b2"].reshape(TPB, CPT, 9)[:, :, :TAPS]
    b2 = np.ascontiguousarray(b2.transpose(1, 0, 2).reshape(1, CPT, TPB * TAPS))
    bias = a["bias"].reshape(TPB, CPT).T
    bias = np.ascontiguousarray(np.concatenate([bias, bias[:, :2]], axis=1))
    arrays = {"x": np.ascontiguousarray(a["x"]), "w1": w1, "gamma": a["gamma"], "beta": a["beta"],
              "mean": a["running_mean"], "var": a["running_var"], "w2": w2, "b2": b2, "bias": bias}

    nc = bacc.Bacc("TRN2", target_bir_lowering=False, num_devices=1)
    aps = [nc.dram_tensor(f"{k}_dram", v.shape, mybir.dt.from_np(v.dtype), kind="ExternalInput").ap()
           for k, v in arrays.items()]
    out = nc.dram_tensor("out_dram", _OUT, F32, kind="ExternalOutput").ap()
    conv_kernel(nc, *aps, out)
    r = run_bass_kernel_spmd(nc, [{f"{k}_dram": v for k, v in arrays.items()}], core_ids=[0])
    return r.results[0]["out_dram"]
```

```python
from contextlib import ExitStack

import numpy as np

import concourse.bass as bass
from concourse import mybir

F32 = mybir.dt.float32
U8 = mybir.dt.uint8
ALU = mybir.AluOpType
ACT = mybir.ActivationFunctionType

B, C, H, W = 4, 192, 256, 256
HID = C // 4
TAPS = 4
EPS = 1e-5
P = 128
ROWS = 8
BLK = H // ROWS
CPT = P // BLK
TPB = C // CPT
FREE = ROWS * W

STEPS = 4
GROUPS = TPB // STEPS
RES = 18
RP = 2
RC = 4
HALF = ROWS // 2
RO = 2
RO_LAST = RO + RP
RX_LAST = RES - RP + RC
STREAM = TPB - RES
NMAT = 6

CHAIN_GROUPS = 2
SPENT = TPB - CHAIN_GROUPS * STEPS
EARLY = RO
ITEMS = {"first": [2] + [6] * 4 + [4] * 5 + [0] * CHAIN_GROUPS,
         "middle": [2] + [6] * 5 + [4] * 4 + [0] * CHAIN_GROUPS,
         "last": [0] * GROUPS}
FIRST = {k: [(EARLY if k == "first" else 0) + sum(v[:g]) for g in range(GROUPS + 1)] for k, v in ITEMS.items()}
assert FIRST["first"][-1] == FIRST["middle"][-1] == TPB

FIRST_IN = [RES + (s - RES) % RC for s in range(RC)]
PER_SLOT = [len(range(t, TPB, RC)) for t in FIRST_IN]

CYCLES = 4
CYCLE, CYCLE_LOADS = TPB // CYCLES, 2 * STEPS
assert (RES - RP) % STEPS == 0 and CYCLES * CYCLE_LOADS + RES >= TPB


def spread(items):
    return [list(range(items * s // STEPS, items * (s + 1) // STEPS)) for s in range(STEPS)]


def place(t):
    return sum(t >= edge for edge in (RES, RES + RC, RES + RC + RX_LAST))


def runs(batch):
    def kind(g):
        places = [place(g * STEPS + s) for s in range(STEPS)]
        if batch == "last":
            return ("alone", g) if g in (0, GROUPS - 1) else places
        lo, hi = FIRST[batch][g] + RP - 1, FIRST[batch][g + 1] + RP - 1
        if g == 0 or ITEMS[batch][g] == 0 or hi > TPB or lo < STREAM < hi:
            return ("alone", g)
        return (ITEMS[batch][g], lo >= STREAM, [min(p, 2) for p in places])
    out, g = [], 0
    while g < GROUPS:
        e = g + 1
        while e < GROUPS and kind(e) == kind(g):
            e += 1
        out.append((g, e))
        g = e
    return out


def conv_kernel(nc, x, w1, gamma, beta, mean, var, w2, b2, bias, out):
    x_t = x.rearrange("b c (k r) w -> (b c k r w)", r=ROWS).rearrange("(g p f) -> g p f", p=P, f=FREE)
    out_t = out.rearrange("b c (k r) w -> (b c k r w)", r=ROWS).rearrange("(g p f) -> g p f", p=P, f=FREE)

    with ExitStack() as ctx:
        def sb(name, shape, dt=F32):
            return ctx.enter_context(nc.sbuf_tensor(name, shape, dt))

        def sem(name):
            return ctx.enter_context(nc.semaphore(name))

        slots = sb("slots", [P, (RES + RC) * FREE])
        resident, conv_ring = slots[:, 0:RES * FREE], slots[:, RES * FREE:]
        out_ring = sb("out_ring", [P, RO * FREE])
        unused = sb("unused", [P, FREE], U8)
        sums = sb("sums", [P, TPB])
        w1_sb = sb("w1_sb", [TPB, CPT, HID])
        w2_sb = sb("w2_sb", [HID + 1, CPT, TPB * TAPS])
        masks = sb("masks", [P, 2 * P])
        mats = sb("mats", [P, 2, NMAT * P])
        taps = sb("taps", [P, (TPB + 2) * TAPS])
        bias_sb = sb("bias_sb", [P, TPB + 2])
        bias_now = sb("bias_now", [P, 2])
        chan = sb("chan", [P, CPT])
        pooled = sb("pooled", [TPB, CPT])
        bn = sb("bn", [HID, 8])
        h_sb = sb("h_sb", [HID + 1, BLK])
        GAMMA, BETA, MEAN, VAR, ROOT, RSTD, VAR_EPS, SHIFT = (bn[:, i:i + 1] for i in range(8))

        conv_ps = [ctx.enter_context(nc.psum_tensor(f"conv_ps{i}", [P, 3 * 512], F32)) for i in range(2)]
        net_ps = ctx.enter_context(nc.psum_tensor("net_ps", [P, 512], F32))
        taps_ps = ctx.enter_context(nc.psum_tensor("taps_ps", [P, 512], F32))

        loaded = [sem(f"loaded{i}") for i in range(RP)]
        reloaded = [sem(f"reloaded{i}") for i in range(RC)]
        stored = [[sem(f"stored_{'AB'[h]}{i}") for h in range(2)] for i in range(RO)]
        stored_last = [[sem(f"stored_last_{'AB'[h]}{i}") for h in range(2)] for i in range(RO_LAST)]
        const_in = sem("const_in")
        masks_set = sem("masks_set")
        chan_set = sem("chan_set")
        bn_set = sem("bn_set")
        bias_set = sem("bias_set")
        summed = sem("summed")
        mats_built = sem("mats_built")
        ps_full = sem("ps_full")
        moved = sem("moved")
        started = sem("started")
        tap2_a = sem("tap2_a")
        tap0_b = sem("tap0_b")
        tap2_b = sem("tap2_b")
        conv_done = sem("conv_done")
        pooled_ps = sem("pooled_ps")
        pooled_sb = sem("pooled_sb")
        hid_ps = sem("hid_ps")
        h_set = sem("h_set")
        taps_full = sem("taps_full")
        taps_set = sem("taps_set")
        taps_rest = sem("taps_rest")

        def rows(t, lo, hi, c0=0, c1=W):
            return t.rearrange("p (r w) -> p r w", w=W)[:, lo:hi, c0:c1]

        def slot(ring, i):
            return ring[:, bass.ds(i * FREE, FREE)]

        def out_half(s, h, last):
            i = s % (RO_LAST if last else RO)
            ring, i = (out_ring, i) if i < RO else (resident, i - RO)
            lo = i * FREE + h * HALF * W
            return ring[:, lo:lo + HALF * W]

        def x_tile(g, s, g0, last):
            where = place(g0 * STEPS + s)
            if where == 0:
                return slot(resident, g * STEPS + s)
            if where == 1 or not last:
                return slot(conv_ring, s)
            return slot(slots, g * STEPS + s - (where - 1) * RX_LAST)

        def tap2_left(s, g0, kind):
            return s % 2 == 1 and not (kind == "last" and g0 == GROUPS - 1)

        def tap(t, k):
            return taps[:, bass.ds(t * TAPS + k, 1)]

        def schedule(eng, group, last_batch=None):
            def batch(b, kind):
                for lo, hi in runs(kind):
                    if hi - lo > 1:
                        with eng.Fori(lo, hi) as g:
                            group(b, g, lo, kind)
                    elif hi - lo == 1:
                        group(b, lo, lo, kind)
            batch(0, "first")
            with eng.Fori(1, B - 1) as b:
                batch(b, "middle")
            if last_batch:
                last_batch()
            else:
                batch(B - 1, "last")

        def item0(i, s, i0):
            if i0 < STREAM - RC:
                return i + RES + RC, slot(conv_ring, s)
            if i0 < TPB - RC:
                return i - (STREAM - RC), slot(resident, i - (STREAM - RC))
            return FIRST_IN[s], slot(conv_ring, s)

        mixed = (STREAM - RC) // RC
        RUNS0 = [(0, mixed), (mixed, mixed + 1), (mixed + 1, TPB // RC - 1), (TPB // RC - 1, TPB // RC)]

        def for_items0(eng, do, lo, hi):
            if hi - lo == 1:
                for s in range(RC):
                    do(lo * RC + s, s, lo * RC + s)
            else:
                with eng.Fori(lo, hi) as g:
                    for s in range(RC):
                        do(g * RC + s, s, lo * RC + s)

        def reloads(b, g, s):
            return 16 * (TPB // RC - 1 + b * PER_SLOT[s] + (g - FIRST_IN[s] // STEPS) + 1)

        block = ctx.enter_context(nc.Block())

        @block.sync
        def _(sp):
            def load0(i, s, i0):
                if i0 >= RC:
                    sp.wait_ge(summed, i - RC + 1)
                tile, dst = item0(i, s, i0)
                sp.dma_start(dst, x_t[tile]).then_inc(reloaded[s], 16)

            for s in range(RC):
                load0(s, s, s)
            sp.dma_start(w1_sb[:, :, :], w1).then_inc(const_in, 16)
            sp.dma_start(w2_sb[0:HID, :, :], w2).then_inc(const_in, 16)
            sp.dma_start(w2_sb[HID:HID + 1, :, :], b2).then_inc(const_in, 16)
            for i, v in enumerate((gamma, beta, mean, var)):
                sp.dma_start(bn[:, i:i + 1], v.rearrange("(r a) -> r a", a=1)).then_inc(const_in, 16)
            for q in range(CPT):
                sp.dma_start(bias_sb[q * BLK:(q + 1) * BLK, :],
                             bias[q:q + 1, :].to_broadcast([BLK, TPB + 2])).then_inc(const_in, 16)
            for lo, hi in RUNS0:
                for_items0(sp, load0, max(lo, 1), hi)

            for j in range(EARLY):
                sp.dma_start(slot(out_ring, j), x_t[TPB + RES + j]).then_inc(loaded[j], 16)

            def store(n, s, last):
                done = stored_last[s] if last else stored[s % RO]
                for h in range(2):
                    sp.wait_ge(conv_done, n * 2 + h + 1)
                    sp.dma_start(out_t[n][:, h * HALF * W:(h + 1) * HALF * W], out_half(s, h, last))\
                      .then_inc(done[h], 16)

            def load_first(b, s):
                sp.dma_start(slot(conv_ring, s), x_t[b * TPB + FIRST_IN[s]]).then_inc(reloaded[s], 16)

            def group(b, g, g0, kind):
                for s in range(STEPS):
                    n = b * TPB + g * STEPS + s
                    if not (kind == "first" and g0 == 0):
                        store(n - RC, s, False)
                    if g0 == 0 and kind != "first":
                        load_first(b, s)
                    elif g0 * STEPS + s >= RES + RC:
                        sp.dma_start(slot(conv_ring, s), x_t[n]).then_inc(reloaded[s], 16)

            def cycle(c, c0):
                b = B - 1
                for k in range(CYCLE):
                    s = k % STEPS
                    store(b * TPB + c * CYCLE + k - RC, s, c0 > 0 or k >= RC)
                    if c0 == 0 and k < RC:
                        load_first(b, s)
                        continue
                    g, g0 = (c_ * (CYCLE_LOADS // STEPS) + k // STEPS + (RES - RP) // STEPS for c_ in (c, c0))
                    if (RP + RC if c0 == 0 else RP) <= k < RP + CYCLE_LOADS and g0 < GROUPS:
                        sp.wait_ge(reloaded[s], reloads(b, g, s) - 16)
                        sp.dma_start(x_tile(g, s, g0, True), x_t[b * TPB + g * STEPS + s]).then_inc(reloaded[s], 16)

            def last_batch():
                cycle(0, 0)
                with sp.Fori(1, CYCLES - 1) as c:
                    cycle(c, 1)
                cycle(CYCLES - 1, CYCLES - 1)
            schedule(sp, group, last_batch=last_batch)
            for s in range(RC):
                store(B * TPB - RC + s, s, True)
            for h in range(2):
                for s in range(RO):
                    sp.wait_ge(stored[s][h], 16 * ((B - 1) * TPB // RO))
                for s in range(RO_LAST):
                    sp.wait_ge(stored_last[s][h], 16 * (TPB // RO_LAST))

        @block.gpsimd
        def _(gp):
            gp.memset(masks[:, :], 0.0).then_inc(masks_set, 1)
            gp.memset(h_sb[:, :], 1.0).then_inc(masks_set, 1)
            gp.wait_ge(masks_set, 2)
            for i in range(2):
                m = masks[:, i * P:(i + 1) * P]
                gp.affine_select(out=m, in_=m, compare_op=ALU.not_equal, fill=1.0, base=i,
                                 pattern=[[-1, P]], channel_multiplier=1).then_inc(masks_set, 1)
            gp.wait_ge(masks_set, 4)
            gp.memset(masks[:, P:2 * P:BLK], 0.0).then_inc(masks_set, 1)
        MASKS_SET = 5
        CONSTS = 16 * (7 + CPT)

        def ready(eng):
            eng.wait_ge(masks_set, MASKS_SET)

        @block.scalar
        def _(act):
            def pool(t, src, before):
                act.wait_ge(summed, before)
                act.activation(unused[:, :], src, ACT.Copy, accum_out=sums[:, bass.ds(t, 1)]).then_inc(summed, 1)

            def pool0(i, s, i0):
                tile, src = item0(i, s, i0)
                ready(act)
                act.wait_ge(reloaded[s], (i - s) * (16 // RC) + 16)
                pool(tile, src, i)

            for_items0(act, pool0, 0, 1)
            act.wait_ge(bn_set, 1)
            act.activation(ROOT, VAR_EPS, ACT.Sqrt).then_inc(bn_set, 1)
            for lo, hi in RUNS0:
                for_items0(act, pool0, max(lo, 1), hi)

            def net_pooled(b):
                act.wait_ge(pooled_ps, b + 1)
                act.activation(pooled[:, :], net_ps[0:TPB, 0:CPT], ACT.Copy, scale=1.0 / (H * W))\
                   .then_inc(pooled_sb, 1)

            def net_hidden(b):
                act.wait_ge(hid_ps, b + 1)
                act.activation(h_sb[0:HID, :], net_ps[0:HID, 8:9].to_broadcast([HID, BLK]), ACT.Relu,
                               scale=GAMMA, bias=SHIFT).then_inc(h_set, 1)

            def net_taps(lo, hi, to):
                return act.activation(taps[:, to * TAPS:(to + hi - lo) * TAPS],
                                      taps_ps[:, lo * TAPS:hi * TAPS], ACT.Copy)

            def build(t, par):
                for k in range(3):
                    last = act.activation(mats[:, par, 2 * k * P:2 * (k + 1) * P], masks[:, :], ACT.Copy,
                                          scale=tap(t, k))
                last.then_inc(mats_built, 1)

            def issue(b, item, parity, is_stream):
                if is_stream:
                    dst, tile = slot(resident, parity), item + RES
                else:
                    dst, tile = slot(resident, item - STREAM), item - STREAM
                    act.wait_ge(conv_done, ((b - 1) * TPB + tile + 1) * 2)
                act.dma_start(dst, x_t[b * TPB + tile]).then_inc(loaded[parity], 16)

            act.wait_ge(bias_set, 2)
            act.wait_ge(bn_set, 10)
            net_pooled(0)
            net_hidden(0)
            act.wait_ge(taps_full, 1)
            net_taps(0, TPB, 0).then_inc(taps_set, 1)
            act.wait_ge(taps_set, 1)
            build(0, 0)
            build(1, 1)
            for j in range(EARLY):
                ready(act)
                act.wait_ge(loaded[j], 16)
                pool(RES + j, slot(out_ring, j), TPB + j)

            def pool_load(b, first, first_item, j):
                ahead = first + j + RP - 1
                item = first_item + j + RP - 1
                if ahead < TPB:
                    act.wait_ge(summed, (b + 1) * TPB + item - RP + 1)
                    issue(b + 1, item, (j + RP - 1) % RP, ahead < STREAM)

            def pool_item(b, first, first_item, j):
                item = first_item + j
                ready(act)
                act.wait_ge(loaded[j % RP], (b * TPB + first_item) * (16 // RP) + 16 * (j // RP + 1))
                if first + j < STREAM:
                    pool(item + RES, slot(resident, j % RP), (b + 1) * TPB + item)
                else:
                    pool(item - STREAM, slot(resident, item - STREAM), (b + 1) * TPB + item)

            def group(b, g, g0, kind):
                last = kind == "last"
                items = spread(ITEMS[kind][g0]) if g0 else [[], [], [0], [1]]
                first = FIRST[kind][g0]
                first_item = first + (g - g0) * ITEMS[kind][g0]
                chain = [s + STEPS * (g0 - (GROUPS - CHAIN_GROUPS)) for s in range(STEPS)]
                for s in range(STEPS):
                    t = g * STEPS + s
                    n = b * TPB + t
                    if len(items[s]) == 2:
                        pool_load(b, first, first_item, items[s][0])
                        pool_item(b, first, first_item, items[s][0])
                        pool_load(b, first, first_item, items[s][1])
                    elif items[s] and g0:
                        pool_load(b, first, first_item, items[s][0])
                    if chain[s] == 2 and not last:
                        net_pooled(b + 1)
                    if chain[s] == 4 and not last:
                        net_hidden(b + 1)
                    xt = x_tile(g, s, g0, last)
                    for h in range(2):
                        if last and g0 > 0:
                            act.wait_ge(stored_last[s][h], g * 16)
                        elif last and s < RO:
                            act.wait_ge(stored[s][h], 16 * ((B - 1) * TPB // RO))
                        elif not last and not (kind == "first" and g0 == 0 and s < RO):
                            act.wait_ge(stored[s % RO][h], (b * TPB + g * STEPS) * (16 // RO) + 16 * (s // RO))
                    if kind == "first" and g0 == 0 and s < RO:
                        act.wait_ge(summed, TPB + s + 1)
                    if last and g0 == 0 and s >= RO:
                        act.wait_ge(conv_done, (b * TPB + s - RO + 1) * 2)
                    if g0 == 0 and s == 3 and kind != "first":
                        act.wait_ge(taps_rest, b)
                    if chain[s] == 5 and not last:
                        act.wait_ge(taps_full, b + 2)
                    if chain[s] == 6 and not last:
                        act.wait_ge(taps_set, b + 2)
                    if not (kind == "first" and g0 == 0 and s < 2):
                        act.wait_ge(bias_set, n + 1)
                    act.wait_ge(ps_full, n + 1)
                    act.activation(out_half(s, 0, last), conv_ps[s % 2][:, W:W + HALF * W], ACT.Identity,
                                   bias=bias_now[:, s % 2:s % 2 + 1]).then_inc(moved, 1)
                    act.activation(out_half(s, 1, last), xt[:, (HALF - 1) * W:(ROWS - 1) * W], ACT.Identity,
                                   scale=tap(t, 1), bias=bias_now[:, s % 2:s % 2 + 1]).then_inc(started, 1)
                    if chain[s] == 5 and not last:
                        net_taps(0, SPENT, 0)
                        net_taps(0, 2, TPB).then_inc(taps_set, 1)
                    if g0 == 0 and s == 2 and kind != "first":
                        net_taps(SPENT, TPB, SPENT).then_inc(taps_rest, 1)
                    if not (last and chain[s] >= 6):
                        build(t + 2, s % 2)
                    if g0 == 0 and not last:
                        if s == 1 or s == 2:
                            act.wait_ge(conv_done, (b * TPB + s) * 2)
                        if s == 1:
                            issue(b + 1, first_item, 0, True)
                        if s > 1:
                            pool_load(b, first, first_item, items[s][0])
                    if items[s] and not last:
                        pool_item(b, first, first_item, items[s][-1])
            schedule(act, group)

        @block.tensor
        def _(pe):
            def mm(out_ap, lhsT, rhs, start, stop):
                return nc.tensor.matmul(out_ap, lhsT, rhs, start=start, stop=stop)

            def warm(count):
                for _ in range(count):
                    mm(conv_ps[0][:, 0:P], masks[:, 0:P], masks[:, 0:P], True, True)

            def net_mean(b):
                ready(pe)
                pe.wait_ge(summed, (b + 1) * TPB)
                mm(net_ps[0:TPB, 0:CPT], sums[:, :], chan[:, :], True, True).then_inc(pooled_ps, 1)

            def net_w1(b):
                ready(pe)
                pe.wait_ge(pooled_sb, b + 1)
                for q in range(CPT):
                    last = mm(net_ps[0:HID, 8:9], w1_sb[:, q, :], pooled[:, q:q + 1], q == 0, q == CPT - 1)
                last.then_inc(hid_ps, 1)

            def net_w2(b):
                ready(pe)
                pe.wait_ge(h_set, b + 1)
                for q in range(CPT):
                    last = mm(taps_ps[q * BLK:(q + 1) * BLK, 0:TPB * TAPS], h_sb[:, :], w2_sb[:, q, :], True, True)
                last.then_inc(taps_full, 1)

            pe.wait_ge(const_in, CONSTS)
            pe.wait_ge(masks_set, MASKS_SET)
            pe.wait_ge(chan_set, 1 + CPT)
            pe.wait_ge(summed, TPB - 2)
            warm(22)
            net_mean(0)
            warm(1)
            net_w1(0)
            warm(1)
            net_w2(0)
            warm(6)

            def group(b, g, g0, kind):
                for s in range(STEPS):
                    n = b * TPB + g * STEPS + s
                    chain = s + STEPS * (g0 - (GROUPS - CHAIN_GROUPS))
                    if kind != "last":
                        if chain == 1:
                            net_mean(b + 1)
                        if chain == 3:
                            net_w1(b + 1)
                        if chain == 5:
                            net_w2(b + 1)
                    ps = conv_ps[s % 2]
                    xt = x_tile(g, s, g0, kind == "last")
                    d0, s0, d1, s1, d2, s2 = (mats[:, s % 2, i * P:(i + 1) * P] for i in range(NMAT))
                    pe.wait_ge(mats_built, n + 1)
                    if g0 * STEPS + s >= RES:
                        pe.wait_ge(reloaded[s], reloads(b, g, s))
                    if not (kind == "first" and g0 == 0 and s < 2):
                        pe.wait_ge(moved, n - 1)
                    mm(ps[:, W:2 * W], s1, xt[:, 7 * W:8 * W], True, False)
                    mm(ps[:, W + 1:2 * W], s0, xt[:, 7 * W:8 * W - 1], False, False)
                    mm(ps[:, W:2 * W - 1], s2, xt[:, 7 * W + 1:8 * W], False, True)
                    for r, k in ((1, 2), (3, 1)):
                        o = ps[:, W + r * W:W + (r + k) * W]
                        mm(o, d1, xt[:, (r - 1) * W:(r + k - 1) * W], True, False)
                        left = r == 3 and tap2_left(s, g0, kind)
                        last = mm(rows(o, 0, k, 1, W), d0, rows(xt, r - 1, r + k - 1, 0, W - 1), False, left)
                        if not left:
                            last = mm(rows(o, 0, k, 0, W - 1), d2, rows(xt, r - 1, r + k - 1, 1, W), False, True)
                    last.then_inc(ps_full, 1)
            schedule(pe, group)

        @block.vector
        def _(dve):
            V = nc.vector
            V.memset(chan[:, :], 0.0).then_inc(chan_set, 1)
            dve.wait_ge(chan_set, 1)
            for q in range(CPT):
                V.memset(chan[q * BLK:(q + 1) * BLK, q:q + 1], 1.0).then_inc(chan_set, 1)
            dve.wait_ge(const_in, CONSTS)
            V.tensor_scalar(VAR_EPS, VAR, EPS, None, ALU.add).then_inc(bn_set, 1)
            dve.wait_ge(bn_set, 2)
            V.reciprocal(RSTD, ROOT).then_inc(bn_set, 1)
            dve.wait_ge(bn_set, 3)
            V.tensor_tensor(ROOT, RSTD, RSTD, ALU.mult).then_inc(bn_set, 1)
            dve.wait_ge(bn_set, 4)
            V.tensor_tensor(ROOT, ROOT, VAR_EPS, ALU.mult).then_inc(bn_set, 1)
            dve.wait_ge(bn_set, 5)
            V.tensor_scalar(ROOT, ROOT, -0.5, 1.5, ALU.mult, ALU.add).then_inc(bn_set, 1)
            dve.wait_ge(bn_set, 6)
            V.tensor_tensor(RSTD, RSTD, ROOT, ALU.mult).then_inc(bn_set, 1)
            dve.wait_ge(bn_set, 7)
            V.tensor_tensor(GAMMA, GAMMA, RSTD, ALU.mult).then_inc(bn_set, 1)
            dve.wait_ge(bn_set, 8)
            V.tensor_tensor(SHIFT, MEAN, GAMMA, ALU.mult).then_inc(bn_set, 1)
            dve.wait_ge(bn_set, 9)
            V.tensor_tensor(SHIFT, BETA, SHIFT, ALU.subtract).then_inc(bn_set, 1)

            def now(t, par):
                V.tensor_copy(bias_now[:, par:par + 1], bias_sb[:, bass.ds(t, 1)]).then_inc(bias_set, 1)

            now(0, 0)
            now(1, 1)

            def add_tap(o, xr, t, k):
                return V.scalar_tensor_tensor(o, xr, tap(t, k), o, ALU.mult, ALU.add)

            def group(b, g, g0, kind):
                for s in range(STEPS):
                    t = g * STEPS + s
                    n = b * TPB + t
                    if g0 == 0 and s == 0:
                        dve.wait_ge(taps_set, b + 1)
                    oa, ob = (out_half(s, h, kind == "last") for h in range(2))
                    xt = x_tile(g, s, g0, kind == "last")
                    dve.wait_ge(started, n + 1)
                    add_tap(rows(ob, 0, HALF, 1, W), rows(xt, HALF - 1, ROWS - 1, 0, W - 1), t, 0)\
                        .then_inc(tap0_b, 1)
                    dve.wait_ge(moved, n + 1)
                    if tap2_left(s, g0, kind):
                        add_tap(rows(oa, 3, 4, 0, W - 1), rows(xt, 2, 3, 1, W), t, 2).then_inc(tap2_a, 1)
                    else:
                        add_tap(rows(oa, 0, HALF, 1, W), rows(xt, 0, HALF, 0, W - 1), t, 3).then_inc(conv_done, 1)
                    dve.wait_ge(tap0_b, n + 1)
                    add_tap(rows(ob, 0, HALF, 0, W - 1), rows(xt, HALF - 1, ROWS - 1, 1, W), t, 2)\
                        .then_inc(tap2_b, 1)
                    if tap2_left(s, g0, kind):
                        dve.wait_ge(tap2_a, b * (TPB // 2) + g * (STEPS // 2) + (s + 1) // 2)
                        add_tap(rows(oa, 0, HALF, 1, W), rows(xt, 0, HALF, 0, W - 1), t, 3).then_inc(conv_done, 1)
                    now(t + 2, s % 2)
                    dve.wait_ge(tap2_b, n + 1)
                    add_tap(rows(ob, 0, HALF, 1, W), rows(xt, HALF, ROWS, 0, W - 1), t, 3).then_inc(conv_done, 1)
            schedule(dve, group)


_OUT = (B, C, H, W)


def kernel(**inputs):
    import concourse.bacc as bacc
    from concourse.bass_utils import run_bass_kernel_spmd

    a = {k.replace("L0_conv_", ""): np.asarray(v) for k, v in inputs.items()}
    w1 = np.ascontiguousarray(a["w1"].T.reshape(TPB, CPT, HID))
    w2 = a["w2"].reshape(TPB, CPT, 9, HID)[:, :, :TAPS, :]
    w2 = np.ascontiguousarray(w2.transpose(3, 1, 0, 2).reshape(HID, CPT, TPB * TAPS))
    b2 = a["b2"].reshape(TPB, CPT, 9)[:, :, :TAPS]
    b2 = np.ascontiguousarray(b2.transpose(1, 0, 2).reshape(1, CPT, TPB * TAPS))
    bias = a["bias"].reshape(TPB, CPT).T
    bias = np.ascontiguousarray(np.concatenate([bias, bias[:, :2]], axis=1))
    arrays = {"x": np.ascontiguousarray(a["x"]), "w1": w1, "gamma": a["gamma"], "beta": a["beta"],
              "mean": a["running_mean"], "var": a["running_var"], "w2": w2, "b2": b2, "bias": bias}

    nc = bacc.Bacc("TRN2", target_bir_lowering=False, num_devices=1)
    aps = [nc.dram_tensor(f"{k}_dram", v.shape, mybir.dt.from_np(v.dtype), kind="ExternalInput").ap()
           for k, v in arrays.items()]
    out = nc.dram_tensor("out_dram", _OUT, F32, kind="ExternalOutput").ap()
    conv_kernel(nc, *aps, out)
    r = run_bass_kernel_spmd(nc, [{f"{k}_dram": v for k, v in arrays.items()}], core_ids=[0])
    return r.results[0]["out_dram"]
```
